# Optimizing a Trainium2 kernel written in Bass

```python
import numpy as np
import jax
import jax.numpy as jnp

def _softmax(x, axis=-1):
    return jax.nn.softmax(x, axis=axis)

def _gelu(x):
    return jax.nn.gelu(x, approximate=True)

def _silu(x):
    return jax.nn.silu(x)

def _sigmoid(x):
    return jax.nn.sigmoid(x)

def _layernorm(x, axis=-1, eps=1e-05):
    m = jnp.mean(x, axis=axis, keepdims=True)
    v = jnp.var(x, axis=axis, keepdims=True)
    return (x - m) / jnp.sqrt(v + eps)

def _scatter_add(tgt, idx, src, axis=0):
    return tgt.at[idx].add(src)

def _segment_sum(src, seg, n):
    return jax.ops.segment_sum(src, seg, n)
kernel_name = 'mk_adj_preln_d1_adj_r2_39692c'

def setup_inputs(seed: int=0):
    np.random.seed(seed)
    _w = jnp.asarray

    def _rec_inputs():
        import jax
        import jax.numpy as jnp
        _gk = jax.random.key(seed)
        x = -0.001547 + 1.001 * jax.random.normal(jax.random.fold_in(_gk, 1), (64, 128, 128), jnp.float32)
        _w = (1.0 + jnp.arange(128, dtype=jnp.float32)) ** (-0.5)
        _w = _w / _w.mean()
        _pij = jnp.clip(0.125 * _w[:, None] * _w[None, :], 0.0, 1.0)
        _a = jax.random.uniform(jax.random.fold_in(_gk, 2), (64, 128, 128)) < _pij
        _a = jnp.logical_or(_a, jnp.swapaxes(_a, -1, -2))
        _a = jnp.logical_or(_a, jnp.eye(128, dtype=bool))
        _af = _a.astype(jnp.float32)
        _af = _af * jax.random.uniform(jax.random.fold_in(_gk, 3), (64, 128, 128), jnp.float32, 0.05, 4.99997)
        adj = _af
        return (x, adj)
    x, adj = _rec_inputs()

    def _L0_gnn_setup():
        import jax, jax.numpy as jnp
        import numpy as np
        B, N, NAB, NF, NG = (8, 128, 128, 128, 64)
        CUTOFF = 5.0
        LN2 = float(np.log(2.0))

        def ssp(x):
            return jax.nn.softplus(x) - LN2
        key = jax.random.key(seed)
        ks = jax.random.split(key, 12)
        r = jax.random.normal(ks[0], (B, N, NAB), dtype=jnp.float32)
        e = jax.random.uniform(ks[1], (B, N, N), dtype=jnp.float32) * CUTOFF
        A = (jax.random.uniform(ks[2], (B, N, N)) < 0.3).astype(jnp.float32)
        s = 0.05
        W1 = jax.random.normal(ks[3], (NF, NG), dtype=jnp.float32) * s
        b1 = jnp.zeros((NF,), jnp.float32)
        W2 = jax.random.normal(ks[4], (NF, NF), dtype=jnp.float32) * s
        b2 = jnp.zeros((NF,), jnp.float32)
        Wa = jax.random.normal(ks[5], (NF, NAB), dtype=jnp.float32) * s
        Wd1 = jax.random.normal(ks[6], (NAB, NF), dtype=jnp.float32) * s
        bd1 = jnp.zeros((NAB,), jnp.float32)
        Wd2 = jax.random.normal(ks[7], (NAB, NAB), dtype=jnp.float32) * s
        bd2 = jnp.zeros((NAB,), jnp.float32)
        return {'r': r, 'e': e, 'A': A, 'W1': W1, 'b1': b1, 'W2': W2, 'b2': b2, 'Wa': Wa, 'Wd1': Wd1, 'bd1': bd1, 'Wd2': Wd2, 'bd2': bd2}
    _L0_gnn_all = _L0_gnn_setup()
    _L0_gnn_in = {k: v for k, v in _L0_gnn_all.items() if k in ('W1', 'b1', 'W2', 'b2', 'Wa', 'Wd1', 'bd1', 'Wd2', 'bd2')}
    del _L0_gnn_all
    return {'x': x, 'adj': adj, 'L0_gnn_W1': _L0_gnn_in['W1'], 'L0_gnn_b1': _L0_gnn_in['b1'], 'L0_gnn_W2': _L0_gnn_in['W2'], 'L0_gnn_b2': _L0_gnn_in['b2'], 'L0_gnn_Wa': _L0_gnn_in['Wa'], 'L0_gnn_Wd1': _L0_gnn_in['Wd1'], 'L0_gnn_bd1': _L0_gnn_in['bd1'], 'L0_gnn_Wd2': _L0_gnn_in['Wd2'], 'L0_gnn_bd2': _L0_gnn_in['bd2']}

def reference(x, adj, L0_gnn_W1, L0_gnn_b1, L0_gnn_W2, L0_gnn_b2, L0_gnn_Wa, L0_gnn_Wd1, L0_gnn_bd1, L0_gnn_Wd2, L0_gnn_bd2):
    import jax
    import jax.numpy as jnp

    def _L0_gnn_ref(r, e, A, W1, b1, W2, b2, Wa, Wd1, bd1, Wd2, bd2):
        import jax, jax.numpy as jnp
        import numpy as np
        B, N, NAB, NF, NG = (8, 128, 128, 128, 64)
        CUTOFF = 5.0
        LN2 = float(np.log(2.0))

        def ssp(x):
            return jax.nn.softplus(x) - LN2
        offsets = jnp.linspace(0.0, CUTOFF, NG, dtype=jnp.float32)
        width = offsets[1] - offsets[0]
        coeff = -0.5 / (width * width)
        diff = e[:, :, :, None] - offsets
        g = jnp.exp(coeff * diff * diff)
        h = ssp(jnp.einsum('bijg,fg->bijf', g, W1) + b1)
        Wf = jnp.einsum('bijf,gf->bijg', h, W2) + b2
        rf = jnp.einsum('bjd,fd->bjf', r, Wa)
        Am = A[:, :, :, None]
        Wf = Wf * Am
        y = jnp.einsum('bjf,bijf->bif', rf, Wf * Am)
        y = ssp(jnp.einsum('bif,df->bid', y, Wd1) + bd1)
        y = jnp.einsum('bid,ed->bie', y, Wd2) + bd2
        return y
    h = jnp.maximum(_layernorm(x, axis=-1), 0.0)
    x = x + _L0_gnn_ref(h, adj, adj, L0_gnn_W1, L0_gnn_b1, L0_gnn_W2, L0_gnn_b2, L0_gnn_Wa, L0_gnn_Wd1, L0_gnn_bd1, L0_gnn_Wd2, L0_gnn_bd2)
    return x

_drawn_inputs = setup_inputs


def setup_inputs(seed=0):
    import zlib

    import numpy as np

    out = dict(_drawn_inputs(seed))
    spreads = {'L0_gnn_b1': (0.0, 0.1),
     'L0_gnn_b2': (0.0, 0.1),
     'L0_gnn_bd1': (0.0, 0.346),
     'L0_gnn_bd2': (0.0, 0.1)}
    factors = {}
    for name, (base, spread) in spreads.items():
        noise = np.random.default_rng([zlib.crc32(name.encode()), seed]).standard_normal(out[name].shape)
        drawn = base * np.exp(spread * noise) if base else spread * noise
        out[name] = jnp.asarray(drawn.astype(out[name].dtype))
    for name, factor in factors.items():
        out[name] = (out[name] * factor).astype(out[name].dtype)
    return out
```

```python
import concourse.bass as bass
from concourse import mybir
from contextlib import ExitStack

B, N, F, M = 64, 128, 128, 64
P = 128
ROWS_PER_TILE = 8
TILES = N // ROWS_PER_TILE
GROUPS = 4
ROWS = N // GROUPS
HALF = GROUPS * N
CHUNK = 4
CHUNKS = B // CHUNK
CUTOFF = 5.0
WIDTH = CUTOFF / (M - 1)
COEFF = -0.5 / (WIDTH * WIDTH)
LN2 = 0.6931471805599453
EXP_CEILING = 2.0 ** 60
EPS = 1e-5


def gnn_kernel(nc, x_t, adj_t, dist_rows, w1_t, w2_t, wa_t, wd1_t, wd2_t, b1, b2, bd1, bd2,
               neg_offsets, selectors, identity, out_t):
    fp32 = mybir.dt.float32
    bf16 = mybir.dt.bfloat16
    ALU = mybir.AluOpType
    ACT = mybir.ActivationFunctionType
    AX = mybir.AxisListType.X

    ctx = ExitStack()
    with ctx:
        def sb(name, shape, dt=fp32):
            return ctx.enter_context(nc.sbuf_tensor(name, shape, dt))

        def ps(name, shape):
            return ctx.enter_context(nc.psum_tensor(name, shape, fp32))

        def sem(name):
            return ctx.enter_context(nc.semaphore(name))

        x_sb = sb("x_sb", [P, B, F])
        y_sb = sb("y_sb", [P, B, F])
        rf_sb = sb("rf_sb", [P, B, F])
        a2_sb = sb("a2_sb", [P, B, N])
        w1_lo = sb("w1_lo", [P, F])
        w1_hi = sb("w1_hi", [P, F])
        w2_sb = sb("w2_sb", [P, F])
        wa_sb = sb("wa_sb", [P, F])
        wd1_sb = sb("wd1_sb", [P, F])
        wd2_sb = sb("wd2_sb", [P, F])
        b1_col = sb("b1_col", [P, 1])
        b1_shift = sb("b1_shift", [P, 1])
        bd1_col = sb("bd1_col", [P, 1])
        bd1_shift = sb("bd1_shift", [P, 1])
        b2_all = sb("b2_all", [P, F])
        bd2_all = sb("bd2_all", [P, F])
        offs_col = sb("offs_col", [P, 1])
        half_col = sb("half_col", [P, 1])
        eps_col = sb("eps_col", [P, 1])
        sel_sb = sb("sel_sb", [3 * ROWS, TILES, P], bf16)
        ident = sb("ident", [P, P])
        mean = sb("mean", [P, B])
        var = sb("var", [P, B])
        rstd = sb("rstd", [P, B])
        dist_in = sb("dist_in", [ROWS, 2, HALF])
        dist_rest = sb("dist_rest", [ROWS, HALF])
        dist_mid = sb("dist_mid", [ROWS, HALF], bf16)
        dist3 = sb("dist3", [3 * ROWS, 2, HALF], bf16)
        sq = sb("sq", [P, 2, HALF])
        gauss = sb("gauss", [P, 2, HALF])
        soft = sb("soft", [P, 2, 2 * HALF])
        h = sb("h", [P, 2, 2 * HALF])
        msg = sb("msg", [P, 2, 2, HALF])
        diag = sb("diag", [P, N, ROWS])

        z_ps = ps("z_ps", [P, 2, 2 * HALF])
        dist_ps = ps("dist_ps", [P, HALF])
        filt_ps = ps("filt_ps", [P, 2, HALF])
        y_ps = ps("y_ps", [P, HALF])

        weights_in = sem("weights_in")
        x_in = [sem(f"x_in{c}") for c in range(4)]
        adj_in = [sem(f"adj_in{c}") for c in range(4)]
        consts_set = sem("consts_set")
        w1_zeroed = sem("w1_zeroed")
        w1_in = sem("w1_in")
        norm_step = sem("norm_step")
        centred_sq = sem("centred_sq")
        std_done = sem("std_done")
        normed = sem("normed")
        a2_done = sem("a2_done")
        xt_ready = sem("xt_ready")
        relu_done = sem("relu_done")
        rf_ready = sem("rf_ready")
        rf_done = sem("rf_done")
        b2_ready = sem("b2_ready")
        b2_done = sem("b2_done")
        dist_loaded = sem("dist_loaded")
        dist_split = sem("dist_split")
        dist_ready = sem("dist_ready")
        sq_done = sem("sq_done")
        gauss_done = sem("gauss_done")
        z_ready = sem("z_ready")
        exp_done = sem("exp_done")
        clamp_done = sem("clamp_done")
        ln_done = sem("ln_done")
        h_done = sem("h_done")
        filt_ready = sem("filt_ready")
        msg_done = sem("msg_done")
        summed = sem("summed")
        y_ready = sem("y_ready")
        y_done = sem("y_done")
        diag_zeroed = sem("diag_zeroed")
        diag_set = sem("diag_set")
        xb_done = sem("xb_done")
        yt_ready = sem("yt_ready")
        yt_done = sem("yt_done")
        zd_ready = sem("zd_ready")
        ed_done = sem("ed_done")
        cd_done = sem("cd_done")
        ld_done = sem("ld_done")
        hd_done = sem("hd_done")
        o_ready = sem("o_ready")
        o_done = sem("o_done")
        out_written = sem("out_written")

        FILT_CREDIT, MSG_CREDIT, Y_CREDIT = 2, 4, 1
        QB = B // 4

        def bank(k):
            return z_ps[:, k // 2, (k % 2) * HALF:(k % 2 + 1) * HALF]

        xt_bank = [bank(0), bank(1)]
        rf_bank = [bank(2), bank(3)]
        b2_bank = [filt_ps[:, 0, :], filt_ps[:, 1, :]]
        xt_buf = [h[:, 0, 0:HALF], h[:, 0, HALF:2 * HALF]]
        yt_buf = [gauss[:, 0, :], gauss[:, 1, :]]
        sd_buf = [soft[:, 0, 0:HALF], soft[:, 0, HALF:2 * HALF]]
        hd_buf = [h[:, 0, 0:HALF], h[:, 0, HALF:2 * HALF]]
        yt_bank, zd_bank = xt_bank, rf_bank
        o_bank = b2_bank

        def chunk(t, g):
            return t[:, g * CHUNK:(g + 1) * CHUNK, :]

        def as_batches(ap):
            return ap.rearrange("p (b f) -> p b f", b=CHUNK)

        block = ctx.enter_context(nc.Block())

        @block.sync
        def _(sp):
            for c in range(4):
                sp.dma_start(x_sb[:, c * QB:(c + 1) * QB, :], x_t[:, c * QB:(c + 1) * QB, :]).then_inc(x_in[c], 16)
            for dst, src in ((wa_sb, wa_t), (w2_sb, w2_t), (wd1_sb, wd1_t), (wd2_sb, wd2_t), (ident, identity),
                             (b1_col, b1), (bd1_col, bd1), (offs_col, neg_offsets)):
                sp.dma_start(dst[:, :], src).then_inc(weights_in, 16)
            sp.dma_start(b2_all[:, :], b2.partition_broadcast(P)).then_inc(weights_in, 16)
            sp.dma_start(bd2_all[:, :], bd2.partition_broadcast(P)).then_inc(weights_in, 16)
            sp.dma_start(sel_sb[:, :, :], selectors).then_inc(weights_in, 16)
            for c in range(4):
                sp.dma_start(a2_sb[:, c * QB:(c + 1) * QB, :], adj_t[:, c * QB:(c + 1) * QB, :]).then_inc(adj_in[c], 16)
            sp.wait_ge(w1_zeroed, 2)
            sp.dma_start(w1_lo[0:M, :], w1_t).then_inc(w1_in, 16)
            sp.dma_start(w1_hi[M:2 * M, :], w1_t).then_inc(w1_in, 16)
            sp.dma_start(dist_in[:, 0, :], dist_rows[:, 0, :]).then_inc(dist_loaded, 16)
            sp.wait_ge(dist_loaded, 16)
            sp.dma_start(dist_in[:, 1, :], dist_rows[:, 1, :]).then_inc(dist_loaded, 16)
            with sp.Fori(2, B) as b:
                sp.wait_ge(dist_split, b)
                sp.dma_start(dist_in[:, b % 2, :], dist_rows[:, b, :]).then_inc(dist_loaded, 16)
            for g in range(CHUNKS):
                sp.wait_ge(o_done, g + 1)
                sp.dma_start(chunk(out_t, g), chunk(x_sb, g)).then_inc(out_written, 16)
            sp.wait_ge(out_written, 16 * CHUNKS)

        WEIGHTS = 16 * 11

        @block.gpsimd
        def _(pool):
            nc.gpsimd.memset(diag[:, :, :], 0.0).then_inc(diag_zeroed, 1)

            def split(b, buf):
                src = dist_in[:, buf, :]
                nc.gpsimd.tensor_copy(dist3[0:ROWS, buf, :], src)
                pool.drain()
                nc.gpsimd.tensor_tensor(dist_rest[:, :], src, dist3[0:ROWS, buf, :], ALU.subtract)
                pool.drain()
                nc.gpsimd.tensor_copy(dist_mid[:, :], dist_rest[:, :])
                pool.drain()
                nc.gpsimd.tensor_copy(dist3[ROWS:2 * ROWS, buf, :], dist_mid[:, :])
                nc.gpsimd.tensor_tensor(dist3[2 * ROWS:3 * ROWS, buf, :], dist_rest[:, :], dist_mid[:, :],
                                        ALU.subtract)
                pool.drain().then_inc(dist_split, 1)

            def set_diag(b, q):
                r = ROWS // 4
                blocks = diag[:, :, :].rearrange("p (c r) s -> p c (r s)", c=GROUPS)
                first = q * r * (ROWS + 1)
                to = blocks[:, :, first:first + (r - 1) * (ROWS + 1) + 1:ROWS + 1]
                nc.gpsimd.tensor_copy(to, a2_sb[:, b, :].rearrange("p (c r) -> p c r", c=GROUPS)
                                      [:, :, q * r:(q + 1) * r]).then_inc(diag_set, 1)

            pool.wait_ge(dist_loaded, 16)
            split(0, 0)
            pool.wait_ge(diag_zeroed, 1)
            pool.wait_ge(a2_done, 4)
            for q in range(4):
                set_diag(0, q)
            pool.wait_ge(dist_loaded, 32)
            pool.wait_ge(dist_split, 1)
            split(1, 1)
            pool.wait_ge(x_in[3], 16)
            pool.wait_ge(normed, 4)
            pool.wait_ge(weights_in, WEIGHTS)
            for g in range(CHUNKS):
                nc.gpsimd.tensor_tensor(chunk(x_sb, g), chunk(x_sb, g),
                                        bd2_all[:, None, :].broadcast_to([P, CHUNK, F]), ALU.add).then_inc(xb_done, 1)
            with pool.Fori(1, B) as b:
                for q in range(4):
                    pool.wait_ge(summed, MSG_CREDIT + 2 * TILES * (b - 1) + 8 * (q + 1))
                    set_diag(b, q)
                    if q == 3:
                        with pool.If(b < B - 1):
                            pool.wait_ge(dist_loaded, 16 * (b + 2))
                            pool.wait_ge(dist_split, b + 1)
                            split(b + 1, (b + 1) % 2)
            pool.sem_inc(dist_split, 1)

        @block.vector
        def _(dve):
            nc.vector.memset(w1_lo[M:2 * M, :], 0.0).then_inc(w1_zeroed, 1)
            nc.vector.memset(w1_hi[0:M, :], 0.0).then_inc(w1_zeroed, 1)
            nc.vector.memset(half_col[:, :], 0.5).then_inc(consts_set, 1)
            nc.vector.memset(eps_col[:, :], EPS).then_inc(consts_set, 1)
            dve.sem_inc(msg_done, FILT_CREDIT)
            dve.sem_inc(y_done, Y_CREDIT)

            step = [0]

            def own(instruction):
                step[0] += 1
                instruction.then_inc(norm_step, 1)
                dve.wait_ge(norm_step, step[0])

            def quarter(t, c):
                return t[:, c * QB:(c + 1) * QB, :]

            def over_features(col):
                return col[:, :, None].broadcast_to([P, QB, F])

            for c in range(4):
                q = slice(c * QB, (c + 1) * QB)
                dve.wait_ge(x_in[c], 16)
                own(nc.vector.tensor_reduce(mean[:, q], quarter(x_sb, c), AX, ALU.add))
                own(nc.vector.tensor_scalar(mean[:, q], mean[:, q], 1.0 / F, None, ALU.mult))
                own(nc.vector.tensor_tensor(quarter(y_sb, c), quarter(x_sb, c), over_features(mean[:, q]), ALU.subtract))
            centred = step[0]
            for c in range(4):
                q = slice(c * QB, (c + 1) * QB)
                dve.wait_ge(centred_sq, c + 1)
                own(nc.vector.tensor_reduce(var[:, q], quarter(rf_sb, c), AX, ALU.add))
            dve.wait_ge(std_done, 1)
            own(nc.vector.reciprocal(rstd[:, :], rstd[:, :]))
            for c in range(4):
                q = slice(c * QB, (c + 1) * QB)
                nc.vector.tensor_tensor(quarter(y_sb, c), quarter(y_sb, c), over_features(rstd[:, q]),
                                        ALU.mult).then_inc(normed, 1)
            dve.wait_ge(weights_in, WEIGHTS)
            own(nc.vector.tensor_scalar(b1_shift[:, :], b1_col[:, :], -LN2, None, ALU.add))
            own(nc.vector.tensor_scalar(bd1_shift[:, :], bd1_col[:, :], -LN2, None, ALU.add))
            for g in range(CHUNKS + 1):
                if g < CHUNKS:
                    dve.wait_ge(rf_ready, g + 1)
                    nc.vector.tensor_copy(chunk(rf_sb, g), as_batches(rf_bank[g % 2])).then_inc(rf_done, 1)
                if g > 0:
                    dve.wait_ge(b2_ready, g)
                    nc.vector.tensor_tensor(chunk(y_sb, g - 1), as_batches(b2_bank[(g - 1) % 2]),
                                            b2_all[:, None, :].broadcast_to([P, CHUNK, F]), ALU.mult).then_inc(b2_done, 1)

            def clamp(tile, buf):
                dve.wait_ge(exp_done, tile + 1)
                nc.vector.tensor_scalar(soft[:, buf, :], soft[:, buf, :], EXP_CEILING, None, ALU.min).then_inc(clamp_done, 1)

            clamp(0, 0)
            with dve.Fori(0, B) as b:
                for n in range(TILES):
                    t = b * TILES + n
                    buf = n % 2
                    dve.wait_ge(ln_done, t + 1)
                    nc.vector.scalar_tensor_tensor(out=h[:, buf, :], in0=z_ps[:, buf, :], scalar=b1_shift[:, 0:1],
                                                   in1=soft[:, buf, :], op0=ALU.add, op1=ALU.max).then_inc(h_done, 1)
                    clamp(t + 1, 1 - buf)
                    for u in range(2):
                        dve.wait_ge(filt_ready, 2 * t + u + 1)
                        dve.wait_ge(summed, 2 * t + u + 1)
                        nc.vector.tensor_tensor(msg[:, buf, u, :].rearrange("p (c f) -> p c f", c=GROUPS),
                                                filt_ps[:, u, :].rearrange("p (c f) -> p c f", c=GROUPS),
                                                rf_sb[:, b, None, :].broadcast_to([P, GROUPS, F]),
                                                ALU.mult).then_inc(msg_done, 1)
                dve.wait_ge(y_ready, b + 1)
                nc.vector.tensor_tensor(y_sb[:, b, :], y_ps[:, 0:F], y_sb[:, b, :], ALU.add).then_inc(y_done, 1)

            for g in range(CHUNKS + 1):
                if g < CHUNKS:
                    s = g % 2
                    dve.wait_ge(ed_done, g + 1)
                    nc.vector.tensor_scalar(sd_buf[s], sd_buf[s], EXP_CEILING, None, ALU.min).then_inc(cd_done, 1)
                    dve.wait_ge(ld_done, g + 1)
                    nc.vector.scalar_tensor_tensor(out=hd_buf[s], in0=zd_bank[s], scalar=bd1_shift[:, 0:1],
                                                   in1=sd_buf[s], op0=ALU.add, op1=ALU.max).then_inc(hd_done, 1)
                if g > 0:
                    dve.wait_ge(o_ready, g)
                    dve.wait_ge(xb_done, CHUNKS)
                    nc.vector.tensor_tensor(chunk(x_sb, g - 1), as_batches(o_bank[(g - 1) % 2]), chunk(x_sb, g - 1),
                                            ALU.add).then_inc(o_done, 1)

        @block.scalar
        def _(act):
            for c in range(4):
                q = slice(c * QB, (c + 1) * QB)
                act.wait_ge(norm_step, 3 * (c + 1))
                nc.scalar.activation(rf_sb[:, q, :], y_sb[:, q, :], ACT.Square).then_inc(centred_sq, 1)
            for c in range(4):
                q = slice(c * QB, (c + 1) * QB)
                act.wait_ge(adj_in[c], 16)
                nc.scalar.activation(a2_sb[:, q, :], a2_sb[:, q, :], ACT.Square).then_inc(a2_done, 1)
            act.wait_ge(norm_step, 16)
            act.wait_ge(consts_set, 2)
            nc.scalar.activation(rstd[:, :], var[:, :], ACT.Sqrt, bias=eps_col[:, 0:1], scale=1.0 / F).then_inc(std_done, 1)
            for g in range(CHUNKS):
                act.wait_ge(xt_ready, g + 1)
                if g >= 2:
                    act.wait_ge(rf_ready, g - 1)
                nc.scalar.activation(xt_buf[g % 2], xt_bank[g % 2], ACT.Relu).then_inc(relu_done, 1)

            def gaussians(tile, buf):
                act.wait_ge(dist_ready, tile + 1)
                nc.scalar.activation(sq[:, buf, :], dist_ps[:, :], ACT.Square, bias=offs_col[:, 0:1]).then_inc(sq_done, 1)
                act.wait_ge(sq_done, tile + 1)
                nc.scalar.activation(gauss[:, buf, :], sq[:, buf, :], ACT.Exp, scale=COEFF).then_inc(gauss_done, 1)

            def exp_z(tile, buf):
                act.wait_ge(z_ready, tile + 1)
                nc.scalar.activation(soft[:, buf, :], z_ps[:, buf, :], ACT.Exp, bias=b1_col[:, 0:1]).then_inc(exp_done, 1)

            act.wait_ge(weights_in, WEIGHTS)
            gaussians(0, 0)
            gaussians(1, 1)
            exp_z(0, 0)
            with act.Fori(0, B) as b:
                for n in range(TILES):
                    t = b * TILES + n
                    buf = n % 2
                    act.wait_ge(clamp_done, t + 1)
                    nc.scalar.activation(soft[:, buf, :], soft[:, buf, :], ACT.Ln, bias=half_col[:, 0:1],
                                         scale=0.5).then_inc(ln_done, 1)
                    exp_z(t + 1, 1 - buf)
                    gaussians(t + 2, buf)

            for g in range(CHUNKS):
                s = g % 2
                act.wait_ge(yt_ready, g + 1)
                if g >= 2:
                    act.wait_ge(zd_ready, g - 1)
                nc.scalar.activation(yt_buf[s], yt_bank[s], ACT.Copy).then_inc(yt_done, 1)
                act.wait_ge(zd_ready, g + 1)
                if g >= 2:
                    act.wait_ge(hd_done, g - 1)
                nc.scalar.activation(sd_buf[s], zd_bank[s], ACT.Exp, bias=bd1_col[:, 0:1]).then_inc(ed_done, 1)
                act.wait_ge(cd_done, g + 1)
                nc.scalar.activation(sd_buf[s], sd_buf[s], ACT.Ln, bias=half_col[:, 0:1], scale=0.5).then_inc(ld_done, 1)

        @block.tensor
        def _(pe):
            pe.sem_inc(summed, MSG_CREDIT)
            pe.wait_ge(weights_in, WEIGHTS)
            for g in range(CHUNKS + 2):
                if g < CHUNKS:
                    if g % 4 == 0:
                        pe.wait_ge(normed, g // 4 + 1)
                    if g >= 2:
                        pe.wait_ge(relu_done, g - 1)
                    for k in range(CHUNK):
                        last = nc.tensor.transpose(xt_bank[g % 2][:, k * N:(k + 1) * N], y_sb[:, g * CHUNK + k, :], ident[:, :])
                    last.then_inc(xt_ready, 1)
                if 1 <= g <= CHUNKS:
                    r = g - 1
                    pe.wait_ge(relu_done, r + 1)
                    if r >= 2:
                        pe.wait_ge(rf_done, r - 1)
                    for k in range(CHUNK):
                        last = nc.tensor.matmul(rf_bank[r % 2][:, k * F:(k + 1) * F], xt_buf[r % 2][:, k * N:(k + 1) * N],
                                                wa_sb[:, :], start=True, stop=True)
                    last.then_inc(rf_ready, 1)
                if g >= 2:
                    v = g - 2
                    pe.wait_ge(rf_done, v + 1)
                    pe.wait_ge(a2_done, v // 4 + 1)
                    if v >= 2:
                        pe.wait_ge(b2_done, v - 1)
                    for k in range(CHUNK):
                        i = v * CHUNK + k
                        last = nc.tensor.matmul(b2_bank[v % 2][:, k * F:(k + 1) * F], a2_sb[:, i, :], rf_sb[:, i, :],
                                                start=True, stop=True)
                    last.then_inc(b2_ready, 1)

            def broadcast(tile, n, parity):
                if not isinstance(tile, int) or tile:
                    pe.wait_ge(sq_done, tile)
                nc.tensor.matmul(dist_ps[:, :], sel_sb[:, n, :], dist3[:, parity, :], start=True, stop=True).then_inc(dist_ready, 1)

            def filter1(tile, buf):
                pe.wait_ge(gauss_done, tile + 1)
                nc.tensor.matmul(z_ps[:, buf, 0:HALF], w1_lo[:, :], gauss[:, buf, :], start=True, stop=True)
                nc.tensor.matmul(z_ps[:, buf, HALF:2 * HALF], w1_hi[:, :], gauss[:, buf, :], start=True, stop=True).then_inc(z_ready, 1)

            pe.wait_ge(w1_in, 32)
            pe.wait_ge(dist_split, 1)
            pe.wait_ge(rf_done, CHUNKS)
            pe.wait_ge(b2_done, CHUNKS)
            broadcast(0, 0, 0)
            broadcast(1, 1, 0)
            filter1(0, 0)
            broadcast(2, 2, 0)
            filter1(1, 1)
            with pe.Fori(0, B) as b:
                for n in range(TILES):
                    t = b * TILES + n
                    buf = n % 2
                    pe.wait_ge(h_done, t + 1)
                    for u in range(2):
                        pe.wait_ge(msg_done, 2 * t + u + 1)
                        for c in range(GROUPS):
                            k = u * HALF + c * N
                            last = nc.tensor.matmul(filt_ps[:, u, c * F:(c + 1) * F], h[:, buf, k:k + N], w2_sb[:, :],
                                                    start=True, stop=True)
                        last.then_inc(filt_ready, 1)
                    filter1(t + 2, buf)
                    if n + 3 < TILES:
                        broadcast(t + 3, n + 3, b % 2)
                    else:
                        if n + 3 == TILES:
                            pe.wait_ge(dist_split, b + 2)
                        broadcast(t + 3, n + 3 - TILES, (b + 1) % 2)
                    if n == 0:
                        pe.wait_ge(y_done, b + 1)
                    if n % 4 == 0:
                        pe.wait_ge(diag_set, 4 * b + n // 4 + 1)
                    for u in range(2):
                        pe.wait_ge(msg_done, FILT_CREDIT + 2 * t + u + 1)
                        for c in range(GROUPS):
                            last = nc.tensor.matmul(y_ps[c * ROWS:(c + 1) * ROWS, 0:F], diag[:, c * ROWS + 2 * n + u, :],
                                                    msg[:, buf, u, c * F:(c + 1) * F],
                                                    start=n == 0 and u == 0, stop=n == TILES - 1 and u == 1)
                        last.then_inc(summed, 1)
                pe.drain().then_inc(y_ready, 1)

            pe.wait_ge(exp_done, B * TILES + 1)
            pe.wait_ge(y_done, Y_CREDIT + B)
            for g in range(CHUNKS + 2):
                if g < CHUNKS:
                    if g >= 2:
                        pe.wait_ge(yt_done, g - 1)
                    for k in range(CHUNK):
                        last = nc.tensor.transpose(yt_bank[g % 2][:, k * N:(k + 1) * N], y_sb[:, g * CHUNK + k, :], ident[:, :])
                    last.then_inc(yt_ready, 1)
                if 1 <= g <= CHUNKS:
                    r = g - 1
                    pe.wait_ge(yt_done, r + 1)
                    if r >= 2:
                        pe.wait_ge(hd_done, r - 1)
                    nc.tensor.matmul(zd_bank[r % 2], wd1_sb[:, :], yt_buf[r % 2], start=True, stop=True).then_inc(zd_ready, 1)
                if g >= 2:
                    v = g - 2
                    pe.wait_ge(hd_done, v + 1)
                    if v >= 2:
                        pe.wait_ge(o_done, v - 1)
                    for k in range(CHUNK):
                        last = nc.tensor.matmul(o_bank[v % 2][:, k * F:(k + 1) * F], hd_buf[v % 2][:, k * N:(k + 1) * N],
                                                wd2_sb[:, :], start=True, stop=True)
                    last.then_inc(o_ready, 1)


def kernel(x, adj, L0_gnn_W1, L0_gnn_b1, L0_gnn_W2, L0_gnn_b2, L0_gnn_Wa, L0_gnn_Wd1, L0_gnn_bd1, L0_gnn_Wd2, L0_gnn_bd2):
    import ml_dtypes
    import numpy as np
    import concourse.bacc as bacc
    from concourse.bass_utils import run_bass_kernel_spmd

    rows = adj.reshape(B, GROUPS, ROWS, N).transpose(2, 0, 1, 3).reshape(ROWS, B, HALF)
    offsets = np.linspace(0.0, CUTOFF, M, dtype=np.float32)
    sel = np.zeros((3, ROWS, TILES, 2, M), np.float32)
    for r in range(ROWS):
        sel[:, r, r // 2, r % 2, :] = 1.0
    arrays = {
        "x_t": x.transpose(1, 0, 2), "adj_t": adj.transpose(2, 0, 1), "dist_rows": rows,
        "w1_t": L0_gnn_W1.T, "w2_t": L0_gnn_W2.T, "wa_t": L0_gnn_Wa.T, "wd1_t": L0_gnn_Wd1.T, "wd2_t": L0_gnn_Wd2.T,
        "b1": L0_gnn_b1.reshape(P, 1), "b2": L0_gnn_b2, "bd1": L0_gnn_bd1.reshape(P, 1), "bd2": L0_gnn_bd2,
        "neg_offsets": np.tile(-offsets, 2).reshape(P, 1),
        "selectors": sel.reshape(3 * ROWS, TILES, P).astype(ml_dtypes.bfloat16),
        "identity": np.eye(P, dtype=np.float32),
    }
    arrays = {k: np.ascontiguousarray(v) for k, v in arrays.items()}
    nc = bacc.Bacc("TRN2", target_bir_lowering=False, num_devices=1)
    args = [nc.dram_tensor(k, v.shape, mybir.dt.from_np(v.dtype), kind="ExternalInput").ap() for k, v in arrays.items()]
    out_t = nc.dram_tensor("out_t", (P, B, F), mybir.dt.float32, kind="ExternalOutput").ap()
    gnn_kernel(nc, *args, out_t)
    got = run_bass_kernel_spmd(nc, [arrays], core_ids=[0]).results[0]["out_t"]
    return np.ascontiguousarray(got.transpose(1, 0, 2))
```

```python
import numpy as np
import concourse.bass as bass
from concourse import mybir
from contextlib import ExitStack

B, N, F, M = 64, 128, 128, 64
P = 128
ROWS_PER_TILE = 8
TILES = N // ROWS_PER_TILE
GROUPS = 4
ROWS = N // GROUPS
HALF = GROUPS * N
CHUNK = 4
CHUNKS = B // CHUNK
CUTOFF = 5.0
OFFSETS = np.arange(M, dtype=np.float32) * np.float32(CUTOFF / (M - 1))
WIDTH = OFFSETS[1] - OFFSETS[0]
COEFF = float(np.float32(-0.5) / (WIDTH * WIDTH))
LN2 = 0.6931471805599453
EXP_CEILING = 2.0 ** 60
SAFE_Z = 40.0
EPS = 1e-5


def gnn_kernel(nc, x_t, adj_t, dist_rows, w1, w1_t, w2_t, wa_t, wd1_t, wd2_t, b1, b2, bd1, bd2,
               neg_offsets, selectors, identity, out_t):
    fp32 = mybir.dt.float32
    bf16 = mybir.dt.bfloat16
    fp32r = mybir.dt.float32r
    ALU = mybir.AluOpType
    ACT = mybir.ActivationFunctionType
    AX = mybir.AxisListType.X

    ctx = ExitStack()
    with ctx:
        def sb(name, shape, dt=fp32):
            return ctx.enter_context(nc.sbuf_tensor(name, shape, dt))

        def ps(name, shape):
            return ctx.enter_context(nc.psum_tensor(name, shape, fp32))

        def sem(name):
            return ctx.enter_context(nc.semaphore(name))

        x_sb = sb("x_sb", [P, B, F])
        y_sb = sb("y_sb", [P, B, F])
        rf_sb = sb("rf_sb", [P, B, F])
        a2_sb = sb("a2_sb", [P, B, N])
        w1_sb = sb("w1_sb", [P, F])
        w1_high = sb("w1_high", [P, F], fp32r)
        w1_low = sb("w1_low", [P, F], fp32r)
        w1_nat = sb("w1_nat", [P, M])
        w1_abs = sb("w1_abs", [P, M])
        z_bound = sb("z_bound", [P, 2])
        z_most = sb("z_most", [1, 1])
        z_safe = sb("z_safe", [1, 1], mybir.dt.int32)
        w2_sb = sb("w2_sb", [P, F])
        wa_sb = sb("wa_sb", [P, F])
        wd1_sb = sb("wd1_sb", [P, F])
        wd2_sb = sb("wd2_sb", [P, F])
        b1_col = sb("b1_col", [P, 1])
        b1_shift = sb("b1_shift", [P, 1])
        bd1_col = sb("bd1_col", [P, 1])
        bd1_shift = sb("bd1_shift", [P, 1])
        b2_all = sb("b2_all", [P, F])
        bd2_all = sb("bd2_all", [P, F])
        offs_col = sb("offs_col", [P, 1])
        half_col = sb("half_col", [P, 1])
        eps_col = sb("eps_col", [P, 1])
        sel_sb = sb("sel_sb", [3 * ROWS, TILES, P], bf16)
        ident = sb("ident", [P, P])
        mean = sb("mean", [P, B])
        var = sb("var", [P, B])
        rstd = sb("rstd", [P, B])
        dist_in = sb("dist_in", [ROWS, 2, HALF])
        dist_rest = sb("dist_rest", [ROWS, HALF])
        dist_mid = sb("dist_mid", [ROWS, HALF], bf16)
        dist3 = sb("dist3", [3 * ROWS, 2, HALF], bf16)
        sq = sb("sq", [P, 2, HALF])
        gauss = sb("gauss", [P, 2, HALF])
        parts = sb("parts", [P, 2, 2, HALF], fp32r)
        soft = sb("soft", [P, 2, 2 * HALF])
        h = sb("h", [P, 2, 2 * HALF])
        msg = sb("msg", [P, 2, 2, HALF])
        diag = sb("diag", [P, N, ROWS])

        z_ps = ps("z_ps", [P, 2, 2 * HALF])
        dist_ps = ps("dist_ps", [P, HALF])
        filt_ps = ps("filt_ps", [P, 2, HALF])
        y_ps = ps("y_ps", [P, HALF])

        weights_in = sem("weights_in")
        x_in = [sem(f"x_in{c}") for c in range(4)]
        adj_in = [sem(f"adj_in{c}") for c in range(4)]
        consts_set = sem("consts_set")
        bound_ready = sem("bound_ready")
        bound_row = sem("bound_row")
        flag_set = sem("flag_set")
        norm_step = sem("norm_step")
        centred_sq = sem("centred_sq")
        std_done = sem("std_done")
        normed = sem("normed")
        a2_done = sem("a2_done")
        xt_ready = sem("xt_ready")
        relu_done = sem("relu_done")
        rf_ready = sem("rf_ready")
        rf_done = sem("rf_done")
        b2_ready = sem("b2_ready")
        b2_done = sem("b2_done")
        dist_loaded = sem("dist_loaded")
        dist_split = sem("dist_split")
        dist_ready = sem("dist_ready")
        sq_done = sem("sq_done")
        gauss_done = sem("gauss_done")
        high_done = sem("high_done")
        parts_done = sem("parts_done")
        z_ready = sem("z_ready")
        exp_done = sem("exp_done")
        clamp_done = sem("clamp_done")
        ln_done = sem("ln_done")
        h_done = sem("h_done")
        filt_ready = sem("filt_ready")
        msg_done = sem("msg_done")
        summed = sem("summed")
        y_done = sem("y_done")
        diag_zeroed = sem("diag_zeroed")
        diag_set = sem("diag_set")
        xb_done = sem("xb_done")
        yt_ready = sem("yt_ready")
        yt_done = sem("yt_done")
        zd_ready = sem("zd_ready")
        ed_done = sem("ed_done")
        cd_done = sem("cd_done")
        ld_done = sem("ld_done")
        hd_done = sem("hd_done")
        o_ready = sem("o_ready")
        o_done = sem("o_done")
        out_written = sem("out_written")

        FILT_CREDIT, MSG_CREDIT, Y_CREDIT = 2, 4, 1
        QB = B // 4

        def bank(k):
            return z_ps[:, k // 2, (k % 2) * HALF:(k % 2 + 1) * HALF]

        xt_bank = [bank(0), bank(1)]
        rf_bank = [bank(2), bank(3)]
        b2_bank = [filt_ps[:, 0, :], filt_ps[:, 1, :]]
        xt_buf = [h[:, 0, 0:HALF], h[:, 0, HALF:2 * HALF]]
        yt_buf = [gauss[:, 0, :], gauss[:, 1, :]]
        sd_buf = [soft[:, 0, 0:HALF], soft[:, 0, HALF:2 * HALF]]
        hd_buf = [h[:, 0, 0:HALF], h[:, 0, HALF:2 * HALF]]
        yt_bank, zd_bank = xt_bank, rf_bank
        o_bank = b2_bank

        def chunk(t, g):
            return t[:, g * CHUNK:(g + 1) * CHUNK, :]

        def as_batches(ap):
            return ap.rearrange("p (b f) -> p b f", b=CHUNK)

        block = ctx.enter_context(nc.Block())

        @block.sync
        def _(sp):
            for c in range(4):
                sp.dma_start(x_sb[:, c * QB:(c + 1) * QB, :], x_t[:, c * QB:(c + 1) * QB, :]).then_inc(x_in[c], 16)
            for dst, src in ((wa_sb, wa_t), (w2_sb, w2_t), (wd1_sb, wd1_t), (wd2_sb, wd2_t), (ident, identity),
                             (b1_col, b1), (bd1_col, bd1), (offs_col, neg_offsets)):
                sp.dma_start(dst[:, :], src).then_inc(weights_in, 16)
            sp.dma_start(b2_all[:, :], b2.partition_broadcast(P)).then_inc(weights_in, 16)
            sp.dma_start(bd2_all[:, :], bd2.partition_broadcast(P)).then_inc(weights_in, 16)
            sp.dma_start(w1_nat[:, :], w1).then_inc(weights_in, 16)
            sp.dma_start(w1_sb[0:M, :], w1_t).then_inc(weights_in, 16)
            sp.dma_start(w1_sb[M:2 * M, :], w1_t).then_inc(weights_in, 16)
            sp.dma_start(sel_sb[:, :, :], selectors).then_inc(weights_in, 16)
            for c in range(4):
                sp.dma_start(a2_sb[:, c * QB:(c + 1) * QB, :], adj_t[:, c * QB:(c + 1) * QB, :]).then_inc(adj_in[c], 16)
            sp.dma_start(dist_in[:, 0, :], dist_rows[:, 0, :]).then_inc(dist_loaded, 16)
            sp.wait_ge(dist_loaded, 16)
            sp.dma_start(dist_in[:, 1, :], dist_rows[:, 1, :]).then_inc(dist_loaded, 16)
            with sp.Fori(2, B) as b:
                sp.wait_ge(dist_split, b)
                sp.dma_start(dist_in[:, b % 2, :], dist_rows[:, b, :]).then_inc(dist_loaded, 16)
            for g in range(CHUNKS):
                sp.wait_ge(o_done, g + 1)
                sp.dma_start(chunk(out_t, g), chunk(x_sb, g)).then_inc(out_written, 16)
            sp.wait_ge(out_written, 16 * CHUNKS)

        WEIGHTS = 16 * 14

        @block.gpsimd
        def _(pool):
            nc.gpsimd.memset(diag[:, :, :], 0.0).then_inc(diag_zeroed, 1)

            def split(b, buf):
                src = dist_in[:, buf, :]
                nc.gpsimd.tensor_copy(dist3[0:ROWS, buf, :], src)
                pool.drain()
                nc.gpsimd.tensor_tensor(dist_rest[:, :], src, dist3[0:ROWS, buf, :], ALU.subtract)
                pool.drain()
                nc.gpsimd.tensor_copy(dist_mid[:, :], dist_rest[:, :])
                pool.drain()
                nc.gpsimd.tensor_copy(dist3[ROWS:2 * ROWS, buf, :], dist_mid[:, :])
                nc.gpsimd.tensor_tensor(dist3[2 * ROWS:3 * ROWS, buf, :], dist_rest[:, :], dist_mid[:, :],
                                        ALU.subtract)
                pool.drain().then_inc(dist_split, 1)

            def set_diag(b, q):
                r = ROWS // 4
                blocks = diag[:, :, :].rearrange("p (c r) s -> p c (r s)", c=GROUPS)
                first = q * r * (ROWS + 1)
                to = blocks[:, :, first:first + (r - 1) * (ROWS + 1) + 1:ROWS + 1]
                nc.gpsimd.tensor_copy(to, a2_sb[:, b, :].rearrange("p (c r) -> p c r", c=GROUPS)
                                      [:, :, q * r:(q + 1) * r]).then_inc(diag_set, 1)

            pool.wait_ge(dist_loaded, 16)
            split(0, 0)
            pool.wait_ge(diag_zeroed, 1)
            pool.wait_ge(a2_done, 4)
            for q in range(4):
                set_diag(0, q)
            pool.wait_ge(dist_loaded, 32)
            pool.wait_ge(dist_split, 1)
            split(1, 1)
            pool.wait_ge(x_in[3], 16)
            pool.wait_ge(normed, 4)
            pool.wait_ge(weights_in, WEIGHTS)
            for g in range(CHUNKS):
                nc.gpsimd.tensor_tensor(chunk(x_sb, g), chunk(x_sb, g),
                                        bd2_all[:, None, :].broadcast_to([P, CHUNK, F]), ALU.add).then_inc(xb_done, 1)
            with pool.Fori(1, B) as b:
                for q in range(4):
                    pool.wait_ge(summed, MSG_CREDIT + 2 * TILES * (b - 1) + 8 * (q + 1))
                    set_diag(b, q)
                    if q == 3:
                        with pool.If(b < B - 1):
                            pool.wait_ge(dist_loaded, 16 * (b + 2))
                            pool.wait_ge(dist_split, b + 1)
                            split(b + 1, (b + 1) % 2)
            pool.sem_inc(dist_split, 1)

        @block.vector
        def _(dve):
            nc.vector.memset(half_col[:, :], 0.5).then_inc(consts_set, 1)
            nc.vector.memset(eps_col[:, :], EPS).then_inc(consts_set, 1)
            dve.sem_inc(msg_done, FILT_CREDIT)
            dve.sem_inc(y_done, Y_CREDIT)

            step = [0]

            def own(instruction):
                step[0] += 1
                instruction.then_inc(norm_step, 1)
                dve.wait_ge(norm_step, step[0])

            def quarter(t, c):
                return t[:, c * QB:(c + 1) * QB, :]

            def over_features(col):
                return col[:, :, None].broadcast_to([P, QB, F])

            for c in range(4):
                q = slice(c * QB, (c + 1) * QB)
                dve.wait_ge(x_in[c], 16)
                own(nc.vector.tensor_reduce(mean[:, q], quarter(x_sb, c), AX, ALU.add))
                own(nc.vector.tensor_scalar(mean[:, q], mean[:, q], 1.0 / F, None, ALU.mult))
                own(nc.vector.tensor_tensor(quarter(y_sb, c), quarter(x_sb, c), over_features(mean[:, q]), ALU.subtract))
            centred = step[0]
            for c in range(4):
                q = slice(c * QB, (c + 1) * QB)
                dve.wait_ge(centred_sq, c + 1)
                own(nc.vector.tensor_reduce(var[:, q], quarter(rf_sb, c), AX, ALU.add))
            dve.wait_ge(std_done, 1)
            own(nc.vector.reciprocal(rstd[:, :], rstd[:, :]))
            for c in range(4):
                q = slice(c * QB, (c + 1) * QB)
                nc.vector.tensor_tensor(quarter(y_sb, c), quarter(y_sb, c), over_features(rstd[:, q]),
                                        ALU.mult).then_inc(normed, 1)
            dve.wait_ge(weights_in, WEIGHTS)
            own(nc.vector.tensor_scalar(b1_shift[:, :], b1_col[:, :], -LN2, None, ALU.add))
            own(nc.vector.tensor_scalar(bd1_shift[:, :], bd1_col[:, :], -LN2, None, ALU.add))
            own(nc.vector.tensor_copy(w1_high[:, :], w1_sb[:, :]))
            own(nc.vector.tensor_tensor(w1_low[:, :], w1_sb[:, :], w1_high[:, :].bitcast(fp32), ALU.subtract))
            own(nc.vector.scalar_tensor_tensor(out=w1_abs[:, :], in0=w1_nat[:, :], scalar=-1.0, in1=w1_nat[:, :],
                                               op0=ALU.mult, op1=ALU.max))
            own(nc.vector.scalar_tensor_tensor(out=z_bound[:, 1:2], in0=b1_col[:, :], scalar=-1.0, in1=b1_col[:, :],
                                               op0=ALU.mult, op1=ALU.max))
            own(nc.vector.tensor_reduce(z_bound[:, 0:1], w1_abs[:, :], AX, ALU.add))
            nc.vector.tensor_tensor(z_bound[:, 0:1], z_bound[:, 0:1], z_bound[:, 1:2], ALU.add).then_inc(bound_ready, 1)
            dve.wait_ge(bound_row, 1)
            own(nc.vector.tensor_reduce(z_most[:, :], filt_ps[0:1, 0, 0:P], AX, ALU.max))
            nc.vector.tensor_scalar(z_safe[:, :], z_most[:, :], SAFE_Z, None, ALU.is_le).then_inc(flag_set, 1)
            for g in range(CHUNKS + 1):
                if g < CHUNKS:
                    dve.wait_ge(rf_ready, g + 1)
                    nc.vector.tensor_copy(chunk(rf_sb, g), as_batches(rf_bank[g % 2])).then_inc(rf_done, 1)
                if g > 0:
                    dve.wait_ge(b2_ready, g)
                    nc.vector.tensor_tensor(chunk(y_sb, g - 1), as_batches(b2_bank[(g - 1) % 2]),
                                            b2_all[:, None, :].broadcast_to([P, CHUNK, F]), ALU.mult).then_inc(b2_done, 1)

            def clamp(tile, buf):
                dve.wait_ge(exp_done, tile + 1)
                nc.vector.tensor_scalar(soft[:, buf, :], soft[:, buf, :], EXP_CEILING, None, ALU.min).then_inc(clamp_done, 1)

            def split(tile, buf):
                dve.wait_ge(gauss_done, tile + 1)
                for u in range(2):
                    own_half = slice(u * M, (u + 1) * M)
                    nc.vector.tensor_copy(parts[own_half, buf, u, :], gauss[own_half, buf, :]).then_inc(high_done, 1)
                for u in range(2):
                    own_half, other = slice(u * M, (u + 1) * M), slice((1 - u) * M, (2 - u) * M)
                    dve.wait_ge(high_done, 2 * tile + u + 1)
                    last = nc.vector.tensor_tensor(parts[other, buf, u, :], gauss[own_half, buf, :],
                                                   parts[own_half, buf, u, :].bitcast(fp32), ALU.subtract)
                last.then_inc(parts_done, 1)

            def messages(t, b, buf):
                for u in range(2):
                    dve.wait_ge(filt_ready, 2 * t + u + 1)
                    dve.wait_ge(summed, 2 * t + u + 1)
                    nc.vector.tensor_tensor(msg[:, buf, u, :].rearrange("p (c f) -> p c f", c=GROUPS),
                                            filt_ps[:, u, :].rearrange("p (c f) -> p c f", c=GROUPS),
                                            rf_sb[:, b, None, :].broadcast_to([P, GROUPS, F]),
                                            ALU.mult).then_inc(msg_done, 1)

            def finish_y(b):
                dve.wait_ge(summed, MSG_CREDIT + 2 * TILES * (b + 1))
                nc.vector.tensor_tensor(y_sb[:, b, :], y_ps[:, 0:F], y_sb[:, b, :], ALU.add).then_inc(y_done, 1)

            split(0, 0)
            split(1, 1)
            dve.wait_ge(z_ready, 1)
            split(2, 0)
            dve.wait_ge(flag_set, 1)
            safe = dve.value_load(z_safe[0:1, 0:1], min_val=0, max_val=1)
            with dve.If(safe > 0):
                with dve.Fori(0, B) as b:
                    for n in range(TILES):
                        t = b * TILES + n
                        messages(t, b, n % 2)
                        split(t + 3, (n + 1) % 2)
                    finish_y(b)
            with dve.Else():
                clamp(0, 0)
                with dve.Fori(0, B) as b:
                    for n in range(TILES):
                        t = b * TILES + n
                        buf = n % 2
                        dve.wait_ge(ln_done, t + 1)
                        nc.vector.scalar_tensor_tensor(out=h[:, buf, :], in0=z_ps[:, buf, :], scalar=b1_shift[:, 0:1],
                                                       in1=soft[:, buf, :], op0=ALU.add, op1=ALU.max).then_inc(h_done, 1)
                        clamp(t + 1, 1 - buf)
                        messages(t, b, buf)
                        split(t + 3, 1 - buf)
                    finish_y(b)

            for g in range(CHUNKS + 1):
                if g < CHUNKS:
                    s = g % 2
                    dve.wait_ge(ed_done, g + 1)
                    nc.vector.tensor_scalar(sd_buf[s], sd_buf[s], EXP_CEILING, None, ALU.min).then_inc(cd_done, 1)
                    dve.wait_ge(ld_done, g + 1)
                    nc.vector.scalar_tensor_tensor(out=hd_buf[s], in0=zd_bank[s], scalar=bd1_shift[:, 0:1],
                                                   in1=sd_buf[s], op0=ALU.add, op1=ALU.max).then_inc(hd_done, 1)
                if g > 0:
                    dve.wait_ge(o_ready, g)
                    dve.wait_ge(xb_done, CHUNKS)
                    nc.vector.tensor_tensor(chunk(x_sb, g - 1), as_batches(o_bank[(g - 1) % 2]), chunk(x_sb, g - 1),
                                            ALU.add).then_inc(o_done, 1)

        @block.scalar
        def _(act):
            for c in range(4):
                q = slice(c * QB, (c + 1) * QB)
                act.wait_ge(norm_step, 3 * (c + 1))
                nc.scalar.activation(rf_sb[:, q, :], y_sb[:, q, :], ACT.Square).then_inc(centred_sq, 1)
            for c in range(4):
                q = slice(c * QB, (c + 1) * QB)
                act.wait_ge(adj_in[c], 16)
                nc.scalar.activation(a2_sb[:, q, :], a2_sb[:, q, :], ACT.Square).then_inc(a2_done, 1)
            act.wait_ge(norm_step, 16)
            act.wait_ge(consts_set, 2)
            nc.scalar.activation(rstd[:, :], var[:, :], ACT.Sqrt, bias=eps_col[:, 0:1], scale=1.0 / F).then_inc(std_done, 1)
            for g in range(CHUNKS):
                act.wait_ge(xt_ready, g + 1)
                if g >= 2:
                    act.wait_ge(rf_ready, g - 1)
                nc.scalar.activation(xt_buf[g % 2], xt_bank[g % 2], ACT.Relu).then_inc(relu_done, 1)

            def gaussians(tile, buf):
                act.wait_ge(dist_ready, tile + 1)
                nc.scalar.activation(sq[:, buf, :], dist_ps[:, :], ACT.Square, bias=offs_col[:, 0:1]).then_inc(sq_done, 1)
                act.wait_ge(sq_done, tile + 1)
                nc.scalar.activation(gauss[:, buf, :], sq[:, buf, :], ACT.Exp, scale=COEFF).then_inc(gauss_done, 1)

            def exp_z(tile, buf):
                act.wait_ge(z_ready, tile + 1)
                nc.scalar.activation(soft[:, buf, :], z_ps[:, buf, :], ACT.Exp, bias=b1_col[:, 0:1]).then_inc(exp_done, 1)

            act.wait_ge(weights_in, WEIGHTS)
            nc.scalar.preload_act_table_set("natural_log_exp_and_others")
            gaussians(0, 0)
            gaussians(1, 1)
            act.wait_ge(parts_done, 1)
            gaussians(2, 0)
            act.wait_ge(flag_set, 1)
            safe = act.value_load(z_safe[0:1, 0:1], min_val=0, max_val=1)
            exp_z(0, 0)
            with act.If(safe > 0):
                with act.Fori(0, B) as b:
                    for n in range(TILES):
                        t = b * TILES + n
                        buf = n % 2
                        act.wait_ge(exp_done, t + 1)
                        nc.scalar.activation(h[:, buf, :], soft[:, buf, :], ACT.Ln, bias=half_col[:, 0:1],
                                             scale=0.5).then_inc(h_done, 1)
                        exp_z(t + 1, 1 - buf)
                        gaussians(t + 3, 1 - buf)
            with act.Else():
                with act.Fori(0, B) as b:
                    for n in range(TILES):
                        t = b * TILES + n
                        buf = n % 2
                        act.wait_ge(clamp_done, t + 1)
                        nc.scalar.activation(soft[:, buf, :], soft[:, buf, :], ACT.Ln, bias=half_col[:, 0:1],
                                             scale=0.5).then_inc(ln_done, 1)
                        exp_z(t + 1, 1 - buf)
                        gaussians(t + 3, 1 - buf)

            for g in range(CHUNKS):
                s = g % 2
                act.wait_ge(yt_ready, g + 1)
                if g >= 2:
                    act.wait_ge(zd_ready, g - 1)
                nc.scalar.activation(yt_buf[s], yt_bank[s], ACT.Copy).then_inc(yt_done, 1)
                act.wait_ge(zd_ready, g + 1)
                if g >= 2:
                    act.wait_ge(hd_done, g - 1)
                nc.scalar.activation(sd_buf[s], zd_bank[s], ACT.Exp, bias=bd1_col[:, 0:1]).then_inc(ed_done, 1)
                act.wait_ge(cd_done, g + 1)
                nc.scalar.activation(sd_buf[s], sd_buf[s], ACT.Ln, bias=half_col[:, 0:1], scale=0.5).then_inc(ld_done, 1)

        @block.tensor
        def _(pe):
            pe.sem_inc(summed, MSG_CREDIT)
            pe.wait_ge(weights_in, WEIGHTS)
            pe.wait_ge(bound_ready, 1)
            nc.tensor.matmul(filt_ps[0:1, 0, 0:P], z_bound[:, 0:1], ident[:, :], start=True, stop=True).then_inc(bound_row, 1)
            pe.wait_ge(flag_set, 1)
            for g in range(CHUNKS + 2):
                if g < CHUNKS:
                    if g % 4 == 0:
                        pe.wait_ge(normed, g // 4 + 1)
                    if g >= 2:
                        pe.wait_ge(relu_done, g - 1)
                    for k in range(CHUNK):
                        last = nc.tensor.transpose(xt_bank[g % 2][:, k * N:(k + 1) * N], y_sb[:, g * CHUNK + k, :], ident[:, :])
                    last.then_inc(xt_ready, 1)
                if 1 <= g <= CHUNKS:
                    r = g - 1
                    pe.wait_ge(relu_done, r + 1)
                    if r >= 2:
                        pe.wait_ge(rf_done, r - 1)
                    for k in range(CHUNK):
                        last = nc.tensor.matmul(rf_bank[r % 2][:, k * F:(k + 1) * F], xt_buf[r % 2][:, k * N:(k + 1) * N],
                                                wa_sb[:, :], start=True, stop=True)
                    last.then_inc(rf_ready, 1)
                if g >= 2:
                    v = g - 2
                    pe.wait_ge(rf_done, v + 1)
                    pe.wait_ge(a2_done, v // 4 + 1)
                    if v >= 2:
                        pe.wait_ge(b2_done, v - 1)
                    for k in range(CHUNK):
                        i = v * CHUNK + k
                        last = nc.tensor.matmul(b2_bank[v % 2][:, k * F:(k + 1) * F], a2_sb[:, i, :], rf_sb[:, i, :],
                                                start=True, stop=True)
                    last.then_inc(b2_ready, 1)

            def broadcast(tile, n, parity):
                if not isinstance(tile, int) or tile:
                    pe.wait_ge(sq_done, tile)
                nc.tensor.matmul(dist_ps[:, :], sel_sb[:, n, :], dist3[:, parity, :], start=True, stop=True).then_inc(dist_ready, 1)

            def filter1(tile, buf):
                pe.wait_ge(parts_done, tile + 1)
                for w, first in ((w1_high, True), (w1_low, False)):
                    for u in range(2):
                        last = nc.tensor.matmul(z_ps[:, buf, u * HALF:(u + 1) * HALF], w[:, :], parts[:, buf, u, :],
                                                start=first, stop=not first)
                last.then_inc(z_ready, 1)

            pe.wait_ge(dist_split, 1)
            pe.wait_ge(rf_done, CHUNKS)
            pe.wait_ge(b2_done, CHUNKS)
            broadcast(0, 0, 0)
            broadcast(1, 1, 0)
            broadcast(2, 2, 0)
            filter1(0, 0)
            filter1(1, 1)
            broadcast(3, 3, 0)
            with pe.Fori(0, B) as b:
                for n in range(TILES):
                    t = b * TILES + n
                    buf = n % 2
                    pe.wait_ge(h_done, t + 1)
                    for u in range(2):
                        pe.wait_ge(msg_done, 2 * t + u + 1)
                        for c in range(GROUPS):
                            k = u * HALF + c * N
                            last = nc.tensor.matmul(filt_ps[:, u, c * F:(c + 1) * F], h[:, buf, k:k + N], w2_sb[:, :],
                                                    start=True, stop=True)
                        last.then_inc(filt_ready, 1)
                    filter1(t + 2, buf)
                    if n + 4 < TILES:
                        broadcast(t + 4, n + 4, b % 2)
                    else:
                        if n + 4 == TILES:
                            pe.wait_ge(dist_split, b + 2)
                        broadcast(t + 4, n + 4 - TILES, (b + 1) % 2)
                    if n == 0:
                        pe.wait_ge(y_done, b + 1)
                    if n % 4 == 0:
                        pe.wait_ge(diag_set, 4 * b + n // 4 + 1)
                    for u in range(2):
                        pe.wait_ge(msg_done, FILT_CREDIT + 2 * t + u + 1)
                        for c in range(GROUPS):
                            last = nc.tensor.matmul(y_ps[c * ROWS:(c + 1) * ROWS, 0:F], diag[:, c * ROWS + 2 * n + u, :],
                                                    msg[:, buf, u, c * F:(c + 1) * F],
                                                    start=n == 0 and u == 0, stop=n == TILES - 1 and u == 1)
                        last.then_inc(summed, 1)

            pe.wait_ge(exp_done, B * TILES + 1)
            pe.wait_ge(y_done, Y_CREDIT + B)
            for g in range(CHUNKS + 2):
                if g < CHUNKS:
                    if g >= 2:
                        pe.wait_ge(yt_done, g - 1)
                    for k in range(CHUNK):
                        last = nc.tensor.transpose(yt_bank[g % 2][:, k * N:(k + 1) * N], y_sb[:, g * CHUNK + k, :], ident[:, :])
                    last.then_inc(yt_ready, 1)
                if 1 <= g <= CHUNKS:
                    r = g - 1
                    pe.wait_ge(yt_done, r + 1)
                    if r >= 2:
                        pe.wait_ge(hd_done, r - 1)
                    nc.tensor.matmul(zd_bank[r % 2], wd1_sb[:, :], yt_buf[r % 2], start=True, stop=True).then_inc(zd_ready, 1)
                if g >= 2:
                    v = g - 2
                    pe.wait_ge(hd_done, v + 1)
                    if v >= 2:
                        pe.wait_ge(o_done, v - 1)
                    for k in range(CHUNK):
                        last = nc.tensor.matmul(o_bank[v % 2][:, k * F:(k + 1) * F], hd_buf[v % 2][:, k * N:(k + 1) * N],
                                                wd2_sb[:, :], start=True, stop=True)
                    last.then_inc(o_ready, 1)


def kernel(x, adj, L0_gnn_W1, L0_gnn_b1, L0_gnn_W2, L0_gnn_b2, L0_gnn_Wa, L0_gnn_Wd1, L0_gnn_bd1, L0_gnn_Wd2, L0_gnn_bd2):
    import ml_dtypes
    import concourse.bacc as bacc
    from concourse.bass_utils import run_bass_kernel_spmd

    rows = adj.reshape(B, GROUPS, ROWS, N).transpose(2, 0, 1, 3).reshape(ROWS, B, HALF)
    sel = np.zeros((3, ROWS, TILES, 2, M), np.float32)
    for r in range(ROWS):
        sel[:, r, r // 2, r % 2, :] = 1.0
    arrays = {
        "x_t": x.transpose(1, 0, 2), "adj_t": adj.transpose(2, 0, 1), "dist_rows": rows,
        "w1": L0_gnn_W1, "w1_t": L0_gnn_W1.T, "w2_t": L0_gnn_W2.T, "wa_t": L0_gnn_Wa.T, "wd1_t": L0_gnn_Wd1.T, "wd2_t": L0_gnn_Wd2.T,
        "b1": L0_gnn_b1.reshape(P, 1), "b2": L0_gnn_b2, "bd1": L0_gnn_bd1.reshape(P, 1), "bd2": L0_gnn_bd2,
        "neg_offsets": np.tile(-OFFSETS, 2).reshape(P, 1),
        "selectors": sel.reshape(3 * ROWS, TILES, P).astype(ml_dtypes.bfloat16),
        "identity": np.eye(P, dtype=np.float32),
    }
    arrays = {k: np.ascontiguousarray(v) for k, v in arrays.items()}
    nc = bacc.Bacc("TRN2", target_bir_lowering=False, num_devices=1)
    args = [nc.dram_tensor(k, v.shape, mybir.dt.from_np(v.dtype), kind="ExternalInput").ap() for k, v in arrays.items()]
    out_t = nc.dram_tensor("out_t", (P, B, F), mybir.dt.float32, kind="ExternalOutput").ap()
    gnn_kernel(nc, *args, out_t)
    got = run_bass_kernel_spmd(nc, [arrays], core_ids=[0]).results[0]["out_t"]
    return np.ascontiguousarray(got.transpose(1, 0, 2))
```

```python
import numpy as np
import concourse.bass as bass
from concourse import mybir
from contextlib import ExitStack

B, N, F, M = 64, 128, 128, 64
P = 128
ROWS_PER_TILE = 8
TILES = N // ROWS_PER_TILE
GROUPS = 4
ROWS = N // GROUPS
HALF = GROUPS * N
QUARTERS = 4
QT = TILES // QUARTERS
PAIRS = TILES // 2
CUTOFF = 5.0
OFFSETS = np.arange(M, dtype=np.float32) * np.float32(CUTOFF / (M - 1))
WIDTH = OFFSETS[1] - OFFSETS[0]
COEFF = float(np.float32(-0.5) / (WIDTH * WIDTH))
LN2 = 0.6931471805599453
EXP_CEILING = 2.0 ** 60
SAFE_Z = 40.0
EPS = 1e-5

SLOT_Y, SLOT_HIDDEN, SLOT_X, SLOT_RF, SLOT_OUT = 2, 4, 10, 12, 14
SLOTS = [SLOT_Y, SLOT_HIDDEN, SLOT_X, SLOT_RF, SLOT_OUT]
STEP_STATS, STEP_NORM = 5, 7
STEP_NORM_HELP, STEP_RF_B2 = 5, 13
QUARTER_STEPS = [6, 8, 12, 15]
STEP_EXP, STEP_CEILING, STEP_LN, STEP_SOFTPLUS = 5, 7, 9, 11
DIAG_STEP = ROWS + 1
FIRST_SLOTS = 2

COLUMNS = {"neg_offsets": 1, "b1": 1, "bd1": 1, "w1": M, "w1_t": F, "identity": P, "wa_t": F, "w2_t": F,
           "wd1_t": F, "wd2_t": F, "b2": F, "bd2": F}


def gnn_kernel(nc, x_t, adj_t, distances, weights, out_t):
    fp32 = mybir.dt.float32
    bf16 = mybir.dt.bfloat16
    fp32r = mybir.dt.float32r
    ALU = mybir.AluOpType
    ACT = mybir.ActivationFunctionType
    AX = mybir.AxisListType.X

    ctx = ExitStack()
    with ctx:
        def sb(name, shape, dt=fp32):
            return ctx.enter_context(nc.sbuf_tensor(name, shape, dt))

        def ps(name, shape):
            return ctx.enter_context(nc.psum_tensor(name, shape, fp32))

        def sem(name):
            return ctx.enter_context(nc.semaphore(name))

        weights_sb = sb("weights_sb", [P, sum(COLUMNS.values())])

        def columns_of(name):
            names = list(COLUMNS)
            first = sum(COLUMNS[other] for other in names[:names.index(name)])
            return weights_sb[:, first:first + COLUMNS[name]]

        offs_col = columns_of("neg_offsets")
        b1_col, bd1_col = columns_of("b1"), columns_of("bd1")
        w1_nat = columns_of("w1")
        w1_sb = columns_of("w1_t")
        ident = columns_of("identity")
        wa_sb, w2_sb = columns_of("wa_t"), columns_of("w2_t")
        wd1_sb, wd2_sb = columns_of("wd1_t"), columns_of("wd2_t")
        b2_all, bd2_all = columns_of("b2"), columns_of("bd2")
        w1_abs = sb("w1_abs", [P, M])
        w1_high = sb("w1_high", [P, F], fp32r)
        w1_low = sb("w1_low", [P, F], fp32r)
        b1_shift = sb("b1_shift", [P, 1])
        power_col = sb("power_col", [P, 1])
        z_bound = sb("z_bound", [P, 2])
        z_most = sb("z_most", [1, 1])
        z_safe = sb("z_safe", [1, 1], mybir.dt.int32)
        x_sb = sb("x_sb", [P, 2, F])
        adj_sb = sb("adj_sb", [P, 2, N])
        diag = sb("diag", [P, N * DIAG_STEP])
        stats = sb("stats", [P, 6])
        mean_var = sb("mean_var", [P, 2])
        var_eps = sb("var_eps", [P, 1])
        rstd = sb("rstd", [P, 1])
        xn = sb("xn", [P, F])
        xnt = sb("xnt", [P, N])
        rf = sb("rf", [P, 2, F])
        rf_b2 = sb("rf_b2", [P, F])
        x_bd2 = sb("x_bd2", [P, 4, F])
        y_sb = sb("y_sb", [P, F])
        yt = sb("yt", [P, N])
        zd = sb("zd", [P, N])
        soft_d = sb("soft_d", [P, N])
        hd = sb("hd", [P, N])
        out_sb = sb("out_sb", [P, F])
        dist_wide = sb("dist_wide", [P, QUARTERS, QT, HALF])
        sq = sb("sq", [P, 2, 2, HALF])
        gauss = sb("gauss", [P, 4, HALF])
        parts = sb("parts", [P, 2, 2, HALF], fp32r)
        soft = sb("soft", [P, 2, 2 * HALF])
        h = sb("h", [P, 2, 2 * HALF])
        msg = sb("msg", [P, 4, 2, HALF])

        z_ps = ps("z_ps", [P, 2, 2 * HALF])
        slot_ps = ps("slot_ps", [P, P])
        filt_ps = ps("filt_ps", [P, 2, HALF])
        y_ps = ps("y_ps", [P, HALF])
        first_ps = filt_ps[:, 0, 0:P]
        bound_ps = filt_ps[0:1, 1, 0:P]

        weights_in = sem("weights_in")
        batch_in = sem("batch_in")
        cleared = sem("cleared")
        own_step = sem("own_step")
        bound_ready = sem("bound_ready")
        bound_row = sem("bound_row")
        flag_set = sem("flag_set")
        diag_zeroed = sem("diag_zeroed")
        diag_set = sem("diag_set")
        wide_in = [sem(f"wide_in_{k}") for k in range(QUARTERS)]
        sq_done = sem("sq_done")
        gauss_done = sem("gauss_done")
        high_done = sem("high_done")
        low_done = [sem("low_0_done"), sem("low_1_done")]
        z_ready = sem("z_ready")
        exp_done = sem("exp_done")
        clamp_done = sem("clamp_done")
        ln_done = sem("ln_done")
        h_done = sem("h_done")
        filt_ready = sem("filt_ready")
        msg_done = sem("msg_done")
        summed = sem("summed")
        y_done = sem("y_done")
        slot_ready = sem("slot_ready")
        slot_done = sem("slot_done")
        mean_done = sem("mean_done")
        var_ready = sem("var_ready")
        rstd_done = sem("rstd_done")
        xn_done = sem("xn_done")
        rf_b2_done = sem("rf_b2_done")
        soft_d_exp = sem("soft_d_exp")
        soft_d_cut = sem("soft_d_cut")
        soft_d_ln = sem("soft_d_ln")
        hd_done = sem("hd_done")
        out_written = sem("out_written")

        FILT_CREDIT, MSG_CREDIT, Y_CREDIT, OUT_CREDIT = 2, 8, 1, 32

        def slot_count(b, slot):
            return FIRST_SLOTS + len(SLOTS) * b + SLOTS.index(slot) + 1

        block = ctx.enter_context(nc.Block())

        LOADS = 16 * 2

        @block.sync
        def _(sp):
            def load(b, buf):
                sp.dma_start(x_sb[:, buf, :], x_t[:, b, :]).then_inc(batch_in, 16)
                sp.dma_start(adj_sb[:, buf, :], adj_t[:, b, :]).then_inc(batch_in, 16)

            def load_wide(k, source):
                for u in range(2):
                    sp.dma_start(dist_wide[u * M:(u + 1) * M, k, :, :],
                                 distances[source, k, u, :, :].partition_broadcast(M)).then_inc(wide_in[k], 16)

            def batch(b, following, stores):
                for k in range(QUARTERS):
                    sp.wait_ge(sq_done, PAIRS * b + QT // 2 * (k + 1))
                    load_wide(k, b + 1)
                    if k == 1:
                        sp.wait_ge(diag_set, QUARTERS * (b + 1) + 1)
                        load(following, b % 2)
                if stores:
                    sp.wait_ge(slot_done, slot_count(b, SLOT_OUT))
                    sp.dma_start(out_t[:, b - 1, :], out_sb[:, :]).then_inc(out_written, 16)

            sp.sem_inc(out_written, OUT_CREDIT)
            load_wide(0, 0)
            load(0, 0)
            sp.dma_start(weights_sb[:, :], weights).then_inc(weights_in, 16)
            for k in range(1, QUARTERS):
                load_wide(k, 0)
            sp.wait_ge(batch_in, LOADS)
            load(1, 1)
            batch(0, 2, False)
            with sp.Fori(1, B - 2) as b:
                batch(b, b + 2, True)
            batch(B - 2, B - 1, True)
            for k in range(2):
                sp.wait_ge(sq_done, PAIRS * (B - 1) + QT // 2 * (k + 1))
                load_wide(k, B - 1)
            for b, count in ((B - 1, slot_count(B - 1, SLOT_OUT)), (B, slot_count(B, SLOT_HIDDEN) + 1)):
                sp.wait_ge(slot_done, count)
                sp.dma_start(out_t[:, b - 1, :], out_sb[:, :]).then_inc(out_written, 16)
            sp.wait_ge(out_written, OUT_CREDIT + 16 * B)

        WEIGHTS = 16

        @block.gpsimd
        def _(pool):
            def set_diag(b, q):
                r = ROWS // QUARTERS
                to = diag[:, :].rearrange("p (c r s) -> p c r s", c=GROUPS, r=ROWS)[:, :, q * r:(q + 1) * r, 0]
                a = adj_sb[:, b % 2, :].rearrange("p (c r) -> p c r", c=GROUPS)[:, :, q * r:(q + 1) * r]
                nc.gpsimd.tensor_tensor(to, a, a, ALU.mult).then_inc(diag_set, 1)

            def norm_help(b):
                nc.gpsimd.tensor_tensor(x_bd2[:, b % 4, :], x_sb[:, b % 2, :], bd2_all[:, :], ALU.add)
                pool.wait_ge(var_ready, b + 1)
                nc.gpsimd.tensor_tensor(rstd[:, :], var_eps[:, :], power_col[:, :], ALU.pow).then_inc(rstd_done, 1)

            def rf_by_b2(b, count):
                pool.wait_ge(slot_done, count)
                nc.gpsimd.tensor_tensor(rf_b2[:, :], rf[:, b % 2, :], b2_all[:, :], ALU.mult).then_inc(rf_b2_done, 1)

            def split_low(tile, n, buf):
                pool.wait_ge(high_done, 2 * tile + 2)
                nc.gpsimd.tensor_tensor(parts[0:M, buf, 1, :], gauss[M:2 * M, n % 4, :],
                                        parts[M:2 * M, buf, 1, :].bitcast(fp32), ALU.subtract).then_inc(low_done[1], 1)

            nc.gpsimd.memset(diag[:, :], 0.0).then_inc(diag_zeroed, 1)
            pool.wait_ge(batch_in, LOADS)
            pool.wait_ge(weights_in, WEIGHTS)
            pool.wait_ge(cleared, 3)
            norm_help(0)
            pool.wait_ge(diag_zeroed, 1)
            for q in range(QUARTERS):
                set_diag(0, q)
            pool.drain()
            for tile, buf in ((0, 0), (1, 1), (2, 0)):
                split_low(tile, tile, buf)
            pool.drain()
            rf_by_b2(0, FIRST_SLOTS)
            pool.drain()
            with pool.Fori(0, B) as b:
                for n in range(TILES):
                    split_low(TILES * b + n + 3, n + 3, (n + 1) % 2)
                    others = n in (STEP_NORM_HELP, STEP_RF_B2, *QUARTER_STEPS)
                    if others:
                        pool.drain()
                    if n == STEP_NORM_HELP:
                        pool.wait_ge(batch_in, LOADS * (b + 2))
                        norm_help(b + 1)
                    if n == STEP_RF_B2:
                        rf_by_b2(b + 1, slot_count(b, SLOT_RF))
                    if n in QUARTER_STEPS:
                        q = QUARTER_STEPS.index(n)
                        pool.wait_ge(summed, MSG_CREDIT + 2 * TILES * b + 2 * QT * (q + 1))
                        set_diag(b + 1, q)
                    if others:
                        pool.drain()

        @block.vector
        def _(dve):
            dve.sem_inc(msg_done, FILT_CREDIT)
            dve.sem_inc(y_done, Y_CREDIT)
            nc.vector.memset(y_sb[:, :], 0.0).then_inc(cleared, 1)
            nc.vector.memset(x_bd2[:, 3, :], 0.0).then_inc(cleared, 1)
            nc.vector.memset(power_col[:, :], -0.5).then_inc(cleared, 1)

            def norm_stats(b):
                nc.vector.bn_stats(stats[:, :], x_sb[:, b % 2, :])
                dve.drain()
                nc.vector.bn_aggr(mean_var[:, :], stats[:, :]).then_inc(mean_done, 1)
                dve.wait_ge(mean_done, b + 1)
                nc.vector.tensor_scalar(var_eps[:, :], mean_var[:, 1:2], EPS, None, ALU.add).then_inc(var_ready, 1)

            def normalise(b):
                dve.wait_ge(rstd_done, b + 1)
                nc.vector.tensor_scalar(xn[:, :], x_sb[:, b % 2, :], mean_var[:, 0:1], rstd[:, 0:1],
                                        ALU.subtract, ALU.mult).then_inc(xn_done, 1)

            def take_x(src, count):
                dve.wait_ge(slot_ready, count)
                nc.vector.tensor_scalar(xnt[:, :], src, 0.0, None, ALU.max).then_inc(slot_done, 1)

            def take_rf(b, src, count):
                dve.wait_ge(slot_ready, count)
                nc.vector.tensor_copy(rf[:, b % 2, :], src).then_inc(slot_done, 1)

            def take_y(count):
                dve.wait_ge(slot_ready, count)
                nc.vector.tensor_copy(yt[:, :], slot_ps[:, :]).then_inc(slot_done, 1)

            def take_hidden(count):
                dve.wait_ge(slot_ready, count)
                nc.vector.tensor_scalar(zd[:, :], slot_ps[:, :], bd1_col[:, 0:1], None, ALU.add).then_inc(slot_done, 1)

            def cut_hidden(turn):
                dve.wait_ge(soft_d_exp, turn)
                nc.vector.tensor_scalar(soft_d[:, :], soft_d[:, :], EXP_CEILING, None, ALU.min).then_inc(soft_d_cut, 1)

            def softplus_hidden(turn):
                dve.wait_ge(soft_d_ln, turn)
                nc.vector.scalar_tensor_tensor(out=hd[:, :], in0=zd[:, :], scalar=-LN2, in1=soft_d[:, :],
                                               op0=ALU.add, op1=ALU.max).then_inc(hd_done, 1)

            def take_out(b, count, written):
                dve.wait_ge(slot_ready, count)
                dve.wait_ge(out_written, written)
                nc.vector.tensor_tensor(out_sb[:, :], slot_ps[:, :], x_bd2[:, b % 4, :], ALU.add).then_inc(slot_done, 1)

            def slot(b, n):
                if n == SLOT_Y:
                    take_y(slot_count(b, n))
                if n == SLOT_HIDDEN:
                    take_hidden(slot_count(b, n))
                if n == SLOT_X:
                    take_x(slot_ps[:, :], slot_count(b, n))
                if n == SLOT_RF:
                    take_rf(b + 1, slot_ps[:, :], slot_count(b, n))
                if n == SLOT_OUT:
                    take_out(b + 3, slot_count(b, n), 16 * b + 16)

            def between(b, n):
                if n == STEP_STATS:
                    dve.wait_ge(batch_in, LOADS * (b + 2))
                    norm_stats(b + 1)
                if n == STEP_NORM:
                    normalise(b + 1)
                if n == STEP_CEILING:
                    cut_hidden(b + 1)
                if n == STEP_SOFTPLUS:
                    softplus_hidden(b + 1)

            def clamp(tile, buf):
                dve.wait_ge(exp_done, tile + 1)
                nc.vector.tensor_scalar(soft[:, buf, :], soft[:, buf, :], EXP_CEILING, None, ALU.min).then_inc(clamp_done, 1)

            def split_high(b, n):
                dve.wait_ge(gauss_done, PAIRS * b + n // 2 + 1)
                for u in range(2):
                    own_half = slice(u * M, (u + 1) * M)
                    nc.vector.tensor_copy(parts[own_half, n % 2, u, :], gauss[own_half, n % 4, :]).then_inc(high_done, 1)

            def split_low(tile, n):
                dve.wait_ge(high_done, 2 * tile + 1)
                nc.vector.tensor_tensor(parts[M:2 * M, n % 2, 0, :], gauss[0:M, n % 4, :],
                                        parts[0:M, n % 2, 0, :].bitcast(fp32), ALU.subtract).then_inc(low_done[0], 1)

            def messages(t, b, n):
                buf = n % 4
                slot(b, n)
                dve.wait_ge(z_ready, t + 2)
                split_high(b, n + 3)
                for u in range(2):
                    dve.wait_ge(filt_ready, 2 * t + u + 1)
                    dve.wait_ge(summed, 2 * t + u + 1)
                    nc.vector.tensor_tensor(msg[:, buf, u, :].rearrange("p (c f) -> p c f", c=GROUPS),
                                            filt_ps[:, u, :].rearrange("p (c f) -> p c f", c=GROUPS),
                                            rf[:, b % 2, None, :].broadcast_to([P, GROUPS, F]),
                                            ALU.mult).then_inc(msg_done, 1)

            def take_sum(b):
                dve.wait_ge(summed, MSG_CREDIT + 2 * TILES * (b + 1))
                nc.vector.tensor_copy(y_sb[:, :], y_ps[:, 0:F]).then_inc(y_done, 1)

            steps = [0]

            def own(instruction):
                steps[0] += 1
                instruction.then_inc(own_step, 1)
                dve.wait_ge(own_step, steps[0])

            dve.wait_ge(batch_in, LOADS)
            norm_stats(0)
            dve.wait_ge(weights_in, WEIGHTS)
            own(nc.vector.tensor_copy(w1_high[:, :], w1_sb[:, :]))
            own(nc.vector.tensor_tensor(w1_low[:, :], w1_sb[:, :], w1_high[:, :].bitcast(fp32), ALU.subtract))
            own(nc.vector.scalar_tensor_tensor(out=w1_abs[:, :], in0=w1_nat[:, :], scalar=-1.0, in1=w1_nat[:, :],
                                               op0=ALU.mult, op1=ALU.max))
            own(nc.vector.scalar_tensor_tensor(out=z_bound[:, 1:2], in0=b1_col[:, :], scalar=-1.0, in1=b1_col[:, :],
                                               op0=ALU.mult, op1=ALU.max))
            own(nc.vector.tensor_reduce(z_bound[:, 0:1], w1_abs[:, :], AX, ALU.add))
            nc.vector.tensor_tensor(z_bound[:, 0:1], z_bound[:, 0:1], z_bound[:, 1:2], ALU.add).then_inc(bound_ready, 1)
            own(nc.vector.tensor_scalar(b1_shift[:, :], b1_col[:, :], -LN2, None, ALU.add))
            dve.wait_ge(bound_row, 1)
            own(nc.vector.tensor_reduce(z_most[:, :], bound_ps, AX, ALU.max))
            nc.vector.tensor_scalar(z_safe[:, :], z_most[:, :], SAFE_Z, None, ALU.is_le).then_inc(flag_set, 1)
            split_high(0, 0)
            split_low(0, 0)
            normalise(0)
            split_high(0, 1)
            split_low(1, 1)
            take_x(first_ps, 1)
            take_rf(0, first_ps, 2)
            dve.wait_ge(z_ready, 1)
            split_high(0, 2)
            split_low(2, 2)
            dve.wait_ge(flag_set, 1)
            safe = dve.value_load(z_safe[0:1, 0:1], min_val=0, max_val=1)
            with dve.If(safe > 0):
                with dve.Fori(0, B) as b:
                    for n in range(TILES):
                        t = b * TILES + n
                        messages(t, b, n)
                        split_low(t + 3, n + 3)
                        between(b, n)
                    take_sum(b)
            with dve.Else():
                clamp(0, 0)
                with dve.Fori(0, B) as b:
                    for n in range(TILES):
                        t = b * TILES + n
                        buf = n % 2
                        dve.wait_ge(ln_done, t + 1)
                        nc.vector.scalar_tensor_tensor(out=h[:, buf, :], in0=z_ps[:, buf, :], scalar=b1_shift[:, 0:1],
                                                       in1=soft[:, buf, :], op0=ALU.add, op1=ALU.max).then_inc(h_done, 1)
                        clamp(t + 1, 1 - buf)
                        messages(t, b, n)
                        split_low(t + 3, n + 3)
                        between(b, n)
                    take_sum(b)

            take_y(slot_count(B, SLOT_Y))
            take_hidden(slot_count(B, SLOT_HIDDEN))
            cut_hidden(B + 1)
            softplus_hidden(B + 1)
            take_out(B - 1, slot_count(B, SLOT_HIDDEN) + 1, 16 * B + 16)

        @block.scalar
        def _(act):
            def square(b, n):
                k = n % TILES // QT
                act.wait_ge(wide_in[k], 32 * (b + n // TILES + 1))
                nc.scalar.activation(sq[:, n // 2 % 2, :, :], dist_wide[:, k, n % QT:n % QT + 2, :], ACT.Square,
                                     bias=offs_col[:, 0:1]).then_inc(sq_done, 1)

            def gaussians(b, n):
                act.wait_ge(sq_done, PAIRS * b + n // 2 + 1)
                nc.scalar.activation(gauss[:, n % 4:n % 4 + 2, :], sq[:, n // 2 % 2, :, :], ACT.Exp,
                                     scale=COEFF).then_inc(gauss_done, 1)

            def exp_z(tile, buf):
                act.wait_ge(z_ready, tile + 1)
                nc.scalar.activation(soft[:, buf, :], z_ps[:, buf, :], ACT.Exp, bias=b1_col[:, 0:1]).then_inc(exp_done, 1)

            def exp_hidden(count):
                act.wait_ge(slot_done, count)
                nc.scalar.activation(soft_d[:, :], zd[:, :], ACT.Exp).then_inc(soft_d_exp, 1)

            def ln_hidden(turn):
                act.wait_ge(soft_d_cut, turn)
                nc.scalar.activation(soft_d[:, :], soft_d[:, :], ACT.Ln, bias=0.5,
                                     scale=0.5).then_inc(soft_d_ln, 1)

            def between(b, n):
                if n == STEP_EXP:
                    exp_hidden(slot_count(b, SLOT_HIDDEN))
                if n == STEP_LN:
                    ln_hidden(b + 1)

            nc.scalar.preload_act_table_set("natural_log_exp_and_others")
            act.wait_ge(cleared, 3)
            act.wait_ge(weights_in, WEIGHTS)
            for n in (0, 2):
                square(0, n)
                gaussians(0, n)
            square(0, 4)
            act.wait_ge(flag_set, 1)
            safe = act.value_load(z_safe[0:1, 0:1], min_val=0, max_val=1)
            exp_z(0, 0)
            with act.If(safe > 0):
                with act.Fori(0, B) as b:
                    for n in range(TILES):
                        t = b * TILES + n
                        buf = n % 2
                        act.wait_ge(exp_done, t + 1)
                        nc.scalar.activation(h[:, buf, :], soft[:, buf, :], ACT.Ln, bias=0.5,
                                             scale=0.5).then_inc(h_done, 1)
                        if n % 2 == 1:
                            square(b, n + 5)
                        exp_z(t + 1, 1 - buf)
                        if n % 2 == 0:
                            gaussians(b, n + 4)
                        between(b, n)
            with act.Else():
                with act.Fori(0, B) as b:
                    for n in range(TILES):
                        t = b * TILES + n
                        buf = n % 2
                        act.wait_ge(clamp_done, t + 1)
                        nc.scalar.activation(soft[:, buf, :], soft[:, buf, :], ACT.Ln, bias=0.5,
                                             scale=0.5).then_inc(ln_done, 1)
                        if n % 2 == 1:
                            square(b, n + 5)
                        exp_z(t + 1, 1 - buf)
                        if n % 2 == 0:
                            gaussians(b, n + 4)
                        between(b, n)
            exp_hidden(slot_count(B, SLOT_HIDDEN))
            ln_hidden(B + 1)

        @block.tensor
        def _(pe):
            def filter1(tile, buf):
                for w, first in ((w1_high, True), (w1_low, False)):
                    for u in range(2):
                        if first:
                            pe.wait_ge(low_done[u], tile + 1)
                        last = nc.tensor.matmul(z_ps[:, buf, u * HALF:(u + 1) * HALF], w[:, :], parts[:, buf, u, :],
                                                start=first, stop=not first)
                last.then_inc(z_ready, 1)

            def filter2(t, buf):
                pe.wait_ge(h_done, t + 1)
                for u in range(2):
                    pe.wait_ge(msg_done, 2 * t + u + 1)
                    for c in range(GROUPS):
                        k = u * HALF + c * N
                        last = nc.tensor.matmul(filt_ps[:, u, c * F:(c + 1) * F], h[:, buf, k:k + N], w2_sb[:, :],
                                                start=True, stop=True)
                    last.then_inc(filt_ready, 1)

            def start_sum(b):
                pe.wait_ge(y_done, Y_CREDIT + b)
                pe.wait_ge(rf_b2_done, b + 1)
                pe.wait_ge(diag_set, QUARTERS * (b + 1))
                nc.tensor.matmul(y_ps[:, 0:F], diag[:, 0:N * DIAG_STEP:DIAG_STEP], rf_b2[:, :], start=True, stop=False)

            def add_up(t, n):
                for u in range(2):
                    pe.wait_ge(msg_done, FILT_CREDIT + 2 * t + u + 1)
                    row = 2 * n + u
                    for c in range(GROUPS):
                        columns = c * ROWS * DIAG_STEP + row * ROWS
                        last = nc.tensor.matmul(y_ps[c * ROWS:c * ROWS + row + 1, 0:F],
                                                diag[:, columns:columns + row + 1],
                                                msg[:, n % 4, u, c * F:(c + 1) * F],
                                                start=False, stop=row == ROWS - 1)
                    last.then_inc(summed, 1)

            def transpose_y():
                nc.tensor.transpose(slot_ps[:, :], y_sb[:, :], ident[:, :]).then_inc(slot_ready, 1)

            def hidden():
                nc.tensor.matmul(slot_ps[:, :], wd1_sb[:, :], yt[:, :], start=True, stop=True).then_inc(slot_ready, 1)

            def transpose_x(b, to):
                pe.wait_ge(xn_done, b + 1)
                nc.tensor.transpose(to, xn[:, :], ident[:, :]).then_inc(slot_ready, 1)

            def project(to):
                nc.tensor.matmul(to, xnt[:, :], wa_sb[:, :], start=True, stop=True).then_inc(slot_ready, 1)

            def output(turn):
                pe.wait_ge(hd_done, turn)
                nc.tensor.matmul(slot_ps[:, :], hd[:, :], wd2_sb[:, :], start=True, stop=True).then_inc(slot_ready, 1)

            def slot(b, n):
                if n in SLOTS:
                    pe.wait_ge(slot_done, slot_count(b, n) - 1)
                if n == SLOT_Y:
                    pe.wait_ge(y_done, Y_CREDIT + b)
                    transpose_y()
                if n == SLOT_HIDDEN:
                    hidden()
                if n == SLOT_X:
                    transpose_x(b + 1, slot_ps[:, :])
                if n == SLOT_RF:
                    project(slot_ps[:, :])
                if n == SLOT_OUT:
                    output(b + 1)

            pe.sem_inc(summed, MSG_CREDIT)
            pe.wait_ge(cleared, 3)
            pe.wait_ge(weights_in, WEIGHTS)
            pe.wait_ge(bound_ready, 1)
            nc.tensor.matmul(bound_ps, z_bound[:, 0:1], ident[:, :], start=True, stop=True).then_inc(bound_row, 1)
            filter1(0, 0)
            transpose_x(0, first_ps)
            filter1(1, 1)
            pe.wait_ge(slot_done, 1)
            project(first_ps)
            pe.wait_ge(slot_done, FIRST_SLOTS)
            pe.wait_ge(flag_set, 1)
            with pe.Fori(0, B) as b:
                for n in range(TILES):
                    t = b * TILES + n
                    buf = n % 2
                    slot(b, n)
                    filter2(t, buf)
                    filter1(t + 2, buf)
                    if n == 1:
                        start_sum(b)
                    if n % 2 == 1:
                        add_up(t - 1, n - 1)
                        add_up(t, n)

            pe.wait_ge(y_done, Y_CREDIT + B)
            transpose_y()
            pe.wait_ge(slot_done, slot_count(B, SLOT_Y))
            hidden()
            pe.wait_ge(slot_done, slot_count(B, SLOT_HIDDEN))
            output(B + 1)


def kernel(x, adj, L0_gnn_W1, L0_gnn_b1, L0_gnn_W2, L0_gnn_b2, L0_gnn_Wa, L0_gnn_Wd1, L0_gnn_bd1, L0_gnn_Wd2, L0_gnn_bd2):
    import concourse.bacc as bacc
    from concourse.bass_utils import run_bass_kernel_spmd

    distances = adj.reshape(B, GROUPS, QUARTERS, QT, 2, N).transpose(0, 2, 4, 3, 1, 5).reshape(B, QUARTERS, 2, QT, HALF)
    parts = {
        "neg_offsets": np.tile(-OFFSETS, 2).reshape(P, 1), "b1": L0_gnn_b1.reshape(P, 1), "bd1": L0_gnn_bd1.reshape(P, 1),
        "w1": L0_gnn_W1, "w1_t": np.tile(L0_gnn_W1.T, (2, 1)), "identity": np.eye(P, dtype=np.float32),
        "wa_t": L0_gnn_Wa.T, "w2_t": L0_gnn_W2.T, "wd1_t": L0_gnn_Wd1.T, "wd2_t": L0_gnn_Wd2.T,
        "b2": np.tile(L0_gnn_b2, (P, 1)), "bd2": np.tile(L0_gnn_bd2, (P, 1)),
    }
    arrays = {
        "x_t": x.transpose(1, 0, 2), "adj_t": adj.transpose(2, 0, 1), "distances": distances,
        "weights": np.concatenate([parts[name] for name in COLUMNS], axis=1),
    }
    arrays = {k: np.ascontiguousarray(v) for k, v in arrays.items()}
    nc = bacc.Bacc("TRN2", target_bir_lowering=False, num_devices=1)
    args = [nc.dram_tensor(k, v.shape, mybir.dt.from_np(v.dtype), kind="ExternalInput").ap() for k, v in arrays.items()]
    out_t = nc.dram_tensor("out_t", (P, B, F), mybir.dt.float32, kind="ExternalOutput").ap()
    gnn_kernel(nc, *args, out_t)
    got = run_bass_kernel_spmd(nc, [arrays], core_ids=[0]).results[0]["out_t"]
    return np.ascontiguousarray(got.transpose(1, 0, 2))
```
